# Optimizing a Trainium2 kernel written in Bass

```python
import numpy as np
import jax
import jax.numpy as jnp

def _softmax(x, axis=-1):
    return jax.nn.softmax(x, axis=axis)

def _gelu(x):
    return jax.nn.gelu(x, approximate=True)

def _silu(x):
    return jax.nn.silu(x)

def _sigmoid(x):
    return jax.nn.sigmoid(x)

def _layernorm(x, axis=-1, eps=1e-05):
    m = jnp.mean(x, axis=axis, keepdims=True)
    v = jnp.var(x, axis=axis, keepdims=True)
    return (x - m) / jnp.sqrt(v + eps)

def _scatter_add(tgt, idx, src, axis=0):
    return tgt.at[idx].add(src)

def _segment_sum(src, seg, n):
    return jax.ops.segment_sum(src, seg, n)
kernel_name = 'mk_adj_ffn_d1_adj_r2_b7ce04'

def setup_inputs(seed: int=0):
    np.random.seed(seed)
    _w = jnp.asarray

    def _rec_inputs():
        import jax
        import jax.numpy as jnp
        _gk = jax.random.key(seed)
        x = -0.0005963 + 1.001 * jax.random.normal(jax.random.fold_in(_gk, 1), (2048, 256), jnp.float32)
        _w = (1.0 + jnp.arange(2048, dtype=jnp.float32)) ** (-0.5)
        _w = _w / _w.mean()
        _pij = jnp.clip(0.00390625 * _w[:, None] * _w[None, :], 0.0, 1.0)
        _a = jax.random.uniform(jax.random.fold_in(_gk, 2), (2048, 2048)) < _pij
        _af = _a.astype(jnp.float32)
        adj = _af
        return (x, adj)
    x, adj = _rec_inputs()

    def _L0_gnn_setup():
        import jax, jax.numpy as jnp
        import numpy as np
        N = 3072
        D_IN = 256
        D_OUT = 256
        DENSITY = 0.005
        key = jax.random.key(seed)
        ks = jax.random.split(key, 12)
        x = jax.random.normal(ks[0], (N, D_IN), dtype=jnp.float32)
        adj_a = (jax.random.uniform(ks[1], (N, N)) < DENSITY).astype(jnp.float32)
        adj_b = (jax.random.uniform(ks[2], (N, N)) < DENSITY).astype(jnp.float32)
        W_sa = jax.random.normal(ks[3], (D_IN, D_OUT), dtype=jnp.float32) * (1.414 / np.sqrt(D_IN + D_OUT))
        a_sa = jax.random.normal(ks[4], (1, 2 * D_OUT), dtype=jnp.float32) * (1.414 / np.sqrt(1 + 2 * D_OUT))
        stdv = 1.0 / np.sqrt(D_OUT)
        W_gcnb = jax.random.uniform(ks[5], (D_IN, D_OUT), minval=-stdv, maxval=stdv, dtype=jnp.float32)
        b_gcnb = jax.random.uniform(ks[6], (D_OUT,), minval=-stdv, maxval=stdv, dtype=jnp.float32)
        s = 1.0 / np.sqrt(2 * D_IN)
        Wa = jax.random.uniform(ks[7], (1, 2 * D_IN), minval=-s, maxval=s, dtype=jnp.float32)
        ba = jax.random.uniform(ks[8], (1,), minval=-s, maxval=s, dtype=jnp.float32)
        Wb = jax.random.uniform(ks[9], (1, 2 * D_IN), minval=-s, maxval=s, dtype=jnp.float32)
        bb = jax.random.uniform(ks[10], (1,), minval=-s, maxval=s, dtype=jnp.float32)
        return {'x': x, 'adj_a': adj_a, 'adj_b': adj_b, 'W_sa': W_sa, 'a_sa': a_sa, 'W_gcnb': W_gcnb, 'b_gcnb': b_gcnb, 'Wa': Wa, 'ba': ba, 'Wb': Wb, 'bb': bb}
    _L0_gnn_all = _L0_gnn_setup()
    _L0_gnn_in = {k: v for k, v in _L0_gnn_all.items() if k in ('W_sa', 'a_sa', 'W_gcnb', 'b_gcnb', 'Wa', 'ba', 'Wb', 'bb')}
    del _L0_gnn_all

    def _L0_ffn_setup():
        import jax, jax.numpy as jnp
        import numpy as np
        STEP_SIZE = 0.1

        def _mlp(y, W1, b1, W2, b2, W3, b3):
            h = jnp.tanh(y @ W1.T + b1)
            h = jnp.tanh(h @ W2.T + b2)
            return h @ W3.T + b3

        def _rk4_step(y, dt, params):
            f = lambda z: _mlp(z, *params)
            k1 = f(y)
            k2 = f(y + dt / 2 * k1)
            k3 = f(y + dt / 2 * k2)
            k4 = f(y + dt * k3)
            return y + dt * (k1 + 2 * k2 + 2 * k3 + k4) / 6
        key = jax.random.key(seed)
        ks = jax.random.split(key, 7)
        B, S, D, H = (128, 64, 256, 1024)
        return {'x': jax.random.normal(ks[0], (B, S, D), dtype=jnp.float32), 'W1': jax.random.normal(ks[1], (H, D), dtype=jnp.float32) * (1.0 / np.sqrt(D)), 'b1': jax.random.normal(ks[2], (H,), dtype=jnp.float32) * 0.01, 'W2': jax.random.normal(ks[3], (H, H), dtype=jnp.float32) * (1.0 / np.sqrt(H)), 'b2': jax.random.normal(ks[4], (H,), dtype=jnp.float32) * 0.01, 'W3': jax.random.normal(ks[5], (D, H), dtype=jnp.float32) * (1.0 / np.sqrt(H)), 'b3': jax.random.normal(ks[6], (D,), dtype=jnp.float32) * 0.01}
    _L0_ffn_all = _L0_ffn_setup()
    _L0_ffn_in = {k: v for k, v in _L0_ffn_all.items() if k in ('W1', 'b1', 'W2', 'b2', 'W3', 'b3')}
    del _L0_ffn_all
    return {'x': x, 'adj': adj, 'L0_gnn_W_sa': _L0_gnn_in['W_sa'], 'L0_gnn_a_sa': _L0_gnn_in['a_sa'], 'L0_gnn_W_gcnb': _L0_gnn_in['W_gcnb'], 'L0_gnn_b_gcnb': _L0_gnn_in['b_gcnb'], 'L0_gnn_Wa': _L0_gnn_in['Wa'], 'L0_gnn_ba': _L0_gnn_in['ba'], 'L0_gnn_Wb': _L0_gnn_in['Wb'], 'L0_gnn_bb': _L0_gnn_in['bb'], 'L0_ffn_W1': _L0_ffn_in['W1'], 'L0_ffn_b1': _L0_ffn_in['b1'], 'L0_ffn_W2': _L0_ffn_in['W2'], 'L0_ffn_b2': _L0_ffn_in['b2'], 'L0_ffn_W3': _L0_ffn_in['W3'], 'L0_ffn_b3': _L0_ffn_in['b3']}

def reference(x, adj, L0_gnn_W_sa, L0_gnn_a_sa, L0_gnn_W_gcnb, L0_gnn_b_gcnb, L0_gnn_Wa, L0_gnn_ba, L0_gnn_Wb, L0_gnn_bb, L0_ffn_W1, L0_ffn_b1, L0_ffn_W2, L0_ffn_b2, L0_ffn_W3, L0_ffn_b3):
    import jax
    import jax.numpy as jnp

    def _L0_gnn_ref(x, adj_a, adj_b, W_sa, a_sa, W_gcnb, b_gcnb, Wa, ba, Wb, bb):
        import jax, jax.numpy as jnp
        import numpy as np
        N = 3072
        D_IN = 256
        D_OUT = 256
        DENSITY = 0.005
        type_sum_a = adj_a @ x
        type_sum_b = adj_b @ x
        attn_a = jax.nn.sigmoid(jnp.concatenate([type_sum_a, x], axis=1) @ Wa.T + ba)
        attn_b = jax.nn.sigmoid(jnp.concatenate([type_sum_b, x], axis=1) @ Wb.T + bb)
        h = x @ W_sa
        Hd = h.shape[1]
        s_left = h @ a_sa[0, :Hd]
        s_right = h @ a_sa[0, Hd:]
        scores = s_left[:, None] + s_right[None, :]
        e = jnp.where(adj_a != 0, jnp.exp(-jax.nn.leaky_relu(scores, 0.01)), 0.0)
        attn = e / (jnp.sum(e, axis=1, keepdims=True) + 1e-05)
        x_a = attn @ h
        x_b = adj_b @ (x @ W_gcnb) + b_gcnb
        return jax.nn.sigmoid(attn_a * x_a + attn_b * x_b)

    def _L0_ffn_ref(x, W1, b1, W2, b2, W3, b3):
        import jax, jax.numpy as jnp
        import numpy as np
        STEP_SIZE = 0.1

        def _mlp(y, W1, b1, W2, b2, W3, b3):
            h = jnp.tanh(y @ W1.T + b1)
            h = jnp.tanh(h @ W2.T + b2)
            return h @ W3.T + b3

        def _rk4_step(y, dt, params):
            f = lambda z: _mlp(z, *params)
            k1 = f(y)
            k2 = f(y + dt / 2 * k1)
            k3 = f(y + dt / 2 * k2)
            k4 = f(y + dt * k3)
            return y + dt * (k1 + 2 * k2 + 2 * k3 + k4) / 6
        B, S, D = x.shape
        params = (W1, b1, W2, b2, W3, b3)
        span = 1.0 / (S - 1)
        steps = max(1, int(span / STEP_SIZE))
        dt = span / steps

        def interval(y, _):
            for _s in range(steps):
                y = _rk4_step(y, dt, params)
            return (y, y)
        y0 = x[:, 0]
        _, ys = jax.lax.scan(interval, y0, None, length=S - 1)
        return jnp.concatenate([y0[:, None], jnp.moveaxis(ys, 0, 1)], axis=1)
    x = x + _L0_gnn_ref(_layernorm(x, axis=-1), adj, adj, L0_gnn_W_sa, L0_gnn_a_sa, L0_gnn_W_gcnb, L0_gnn_b_gcnb, L0_gnn_Wa, L0_gnn_ba, L0_gnn_Wb, L0_gnn_bb)
    x = x + _L0_ffn_ref(_layernorm(x, axis=-1)[None], L0_ffn_W1, L0_ffn_b1, L0_ffn_W2, L0_ffn_b2, L0_ffn_W3, L0_ffn_b3)[0]
    return x

_drawn_inputs = setup_inputs


def setup_inputs(seed=0):
    import zlib

    import numpy as np

    out = dict(_drawn_inputs(seed))
    spreads = {}
    factors = {'L0_gnn_a_sa': 3.671,
     'L0_gnn_b_gcnb': 8.0,
     'L0_gnn_Wa': 3.593,
     'L0_ffn_b1': 28.391,
     'L0_ffn_b2': 8.0,
     'L0_ffn_b3': 8.0}
    for name, (base, spread) in spreads.items():
        noise = np.random.default_rng([zlib.crc32(name.encode()), seed]).standard_normal(out[name].shape)
        drawn = base * np.exp(spread * noise) if base else spread * noise
        out[name] = jnp.asarray(drawn.astype(out[name].dtype))
    for name, factor in factors.items():
        out[name] = (out[name] * factor).astype(out[name].dtype)
    return out
```

```python
from contextlib import ExitStack

import concourse.bass as bass
from concourse import mybir

F32 = mybir.dt.float32
F32R = mybir.dt.float32r
I32 = mybir.dt.int32
ALU = mybir.AluOpType
ACT = mybir.ActivationFunctionType
AX = mybir.AxisListType

P = 128
BIG = 3.0e38


class Tally:

    def __init__(self, sem, base=0):
        self.sem, self.base, self.n = sem, base, 0

    def inc(self, ins):
        self.n += 1
        ins.then_inc(self.sem, 1)

    def link(self, eng, ins):
        self.inc(ins)
        eng.wait_ge(self.sem, self.base + self.n)


def graph_stage(nc, x_d, adjT_d, WsaT_d, Wsa_d, a_d, Wg_d, bg_d, wab_d, bab_d, ident_d, x_sb, ident, ones):
    N, D = x_d.shape
    NT = N // P
    DC = D // P
    CH = 256
    NCH = N // CH
    IT = CH // P
    JH = NT // 2
    HC = D + 4
    VC = D + 2

    with ExitStack() as ctx:
        def sb(name, shape, dt=F32):
            return ctx.enter_context(nc.sbuf_tensor(name, shape, dt))

        def sem(name):
            return ctx.enter_context(nc.semaphore(name))

        bank = [ctx.enter_context(nc.psum_tensor(f"gbank{i}", [P, 512], F32)) for i in range(8)]
        xnT = sb("xnT", [P, DC, N])
        wcatH = sb("wcatH", [P, DC, HC])
        wcatV = sb("wcatV", [P, DC, VC])
        wsaT = sb("wsaT", [P, DC, D])
        avec = sb("avec", [P, DC, 2])
        wab = sb("wab", [P, DC, 2, 2])
        bab = sb("bab", [P, 2])
        bg = sb("bg", [P, D])
        stats = sb("stats", [P, NT, 6])
        meanvar = sb("meanvar", [P, NT, 2])
        varc = sb("varc", [P, NT])
        mhalf = sb("mhalf", [P, NT])
        rstd = sb("rstd", [P, NT])
        uleft = sb("uleft", [P, DC, P])
        haug = sb("haug", [P, NT, D + 1])
        vhi = sb("vhi", [P, NT, VC], F32R)
        vlo = sb("vlo", [P, NT, VC], F32R)
        extra = sb("extra", [P, NT, 4])
        negright = sb("negright", [P, NT])
        sleft = sb("sleft", [P, N])
        adj = [sb(f"adj{b}", [P, NT, CH], F32R) for b in range(2)]
        E = [sb(f"E{b}", [P, NT, CH]) for b in range(2)]
        xn = E[0]
        gate = sb("gate", [P, 2])
        gatet = sb("gatet", [P, 2])
        gates = sb("gates", [P, 2])
        rowsum = sb("rowsum", [P, 1])
        rinv = sb("rinv", [P, 1])
        coef = sb("coef", [P, 1])
        xb = sb("xb", [P, D])
        xb2 = sb("xb2", [P, D])
        mixed = sb("mixed", [P, D])
        squash = sb("squash", [P, D])
        half = sb("half", [P, D])

        x_loaded = sem("x_loaded")
        w_loaded = sem("w_loaded")
        adj_loaded = [sem(f"adj_loaded{b}") for b in range(2)]
        prep_step = sem("prep_step")
        var_ready = sem("var_ready")
        rstd_ready = sem("rstd_ready")
        xn_ready = sem("xn_ready")
        u_ready = sem("u_ready")
        wcat_ready = sem("wcat_ready")
        tr_ready = sem("tr_ready")
        tr_copied = sem("tr_copied")
        sl_ready = sem("sl_ready")
        sl_copied = sem("sl_copied")
        hv_ready = sem("hv_ready")
        h_copied = sem("h_copied")
        v_split = sem("v_split")
        negright_ready = sem("negright_ready")
        relu_ready = sem("relu_ready")
        lin_ready = sem("lin_ready")
        exp_ready = sem("exp_ready")
        e_ready = sem("e_ready")
        rows_ready = sem("rows_ready")
        gate_ready = sem("gate_ready")
        gate_squashed = sem("gate_squashed")
        mix_ready = sem("mix_ready")
        mix_squashed = sem("mix_squashed")
        post_step = sem("post_step")
        x2_written = sem("x2_written")

        NW = 8
        TG = 4
        NTG = NT // TG
        block = ctx.enter_context(nc.Block())

        @block.sync
        def _(sp):
            half_n = NT // 2
            xv = x_d.rearrange("(t p) d -> p t d", p=P)
            sp.dma_start(x_sb[:, 0:half_n, :], xv[:, 0:half_n, :]).then_inc(x_loaded, 16)
            sp.dma_start(x_sb[:, half_n:NT, :], xv[:, half_n:NT, :]).then_inc(x_loaded, 16)
            sp.dma_start(wsaT[:, :, :], WsaT_d.rearrange("(c p) f -> p c f", p=P)).then_inc(w_loaded, 16)
            sp.dma_start(avec[:, :, :], a_d).then_inc(w_loaded, 16)
            sp.dma_start(wab[:, :, :, :], wab_d).then_inc(w_loaded, 16)
            sp.dma_start(wcatH[:, :, 0:D], Wsa_d.rearrange("(c p) f -> p c f", p=P)).then_inc(w_loaded, 16)
            sp.dma_start(wcatV[:, :, 0:D], Wg_d.rearrange("(c p) f -> p c f", p=P)).then_inc(w_loaded, 16)
            sp.dma_start(bg[:, :], bg_d).then_inc(w_loaded, 16)
            sp.dma_start(bab[:, :], bab_d).then_inc(w_loaded, 16)
            sp.dma_start(ident[:, :], ident_d).then_inc(w_loaded, 16)

        adjv = adjT_d.rearrange("(t p) i -> p t i", p=P)

        @block.gpsimd
        def _(pool):
            for b in range(2):
                pool.dma_start(adj[b][:, :, :], adjv[:, :, b * CH:(b + 1) * CH]).then_inc(adj_loaded[b], 16)
            pool.wait_ge(var_ready, 1)
            nc.gpsimd.tensor_tensor(rstd[:, :], varc[:, :], mhalf[:, :], ALU.pow).then_inc(rstd_ready, 1)
            with pool.Fori(0, NCH // 2 - 1) as r:
                for b in range(2):
                    pool.wait_ge(rows_ready, r * (2 * IT) + (b + 1) * IT)
                    pool.dma_start(adj[b][:, :, :], adjv[:, :, bass.ds((r * 2 + 2 + b) * CH, CH)])\
                        .then_inc(adj_loaded[b], 16)

        @block.tensor
        def _(pe):
            pe.wait_ge(w_loaded, 16 * NW)
            for c in range(DC):
                for o in range(DC):
                    mm = nc.tensor.matmul(bank[2][:, 2 * c:2 * c + 2], wsaT[:, o, c * P:(c + 1) * P], avec[:, o, :],
                                          start=(o == 0), stop=(o == DC - 1))
            mm.then_inc(u_ready, 1)
            n = 0
            for g in range(NTG):
                pe.wait_ge(xn_ready, TG * (g + 1))
                for c in range(DC):
                    if n >= 2:
                        pe.wait_ge(tr_copied, n - 1)
                    for k in range(TG):
                        mm = nc.tensor.transpose(bank[n % 2][:, k * P:(k + 1) * P],
                                                 xn[:, g * TG + k, c * P:(c + 1) * P], ident[:, :])
                    mm.then_inc(tr_ready, 1)
                    n += 1
            pe.wait_ge(tr_copied, n)
            pe.wait_ge(wcat_ready, 1)
            for q in range(N // 512):
                if q >= 2:
                    pe.wait_ge(sl_copied, q - 1)
                for c in range(DC):
                    mm = nc.tensor.matmul(bank[q % 2][:, :], uleft[:, c, :], xnT[:, c, q * 512:(q + 1) * 512],
                                          start=(c == 0), stop=(c == DC - 1))
                mm.then_inc(sl_ready, 1)
            for t in range(NT):
                if t >= 2:
                    pe.wait_ge(h_copied, t - 1)
                    pe.wait_ge(v_split, t - 1)
                for c in range(DC):
                    nc.tensor.matmul(bank[4 + t % 2][:, 0:HC], xnT[:, c, t * P:(t + 1) * P], wcatH[:, c, :],
                                     start=(c == 0), stop=(c == DC - 1))
                for c in range(DC):
                    mm = nc.tensor.matmul(bank[6 + t % 2][:, 0:VC], xnT[:, c, t * P:(t + 1) * P], wcatV[:, c, :],
                                          start=(c == 0), stop=(c == DC - 1))
                mm.then_inc(hv_ready, 1)
            pe.wait_ge(h_copied, NT)
            pe.wait_ge(v_split, NT)

            def products(chunk, b, rnd):
                pe.wait_ge(adj_loaded[b], rnd * 16 + 16)
                for i in range(IT):
                    first = chunk * IT + i
                    if not (isinstance(chunk, int) and chunk == 0):
                        pe.wait_ge(mix_ready, first + 1 - IT)
                    cols = slice(i * P, (i + 1) * P)
                    for j in range(NT):
                        nc.tensor.matmul(bank[6 + i][:, 0:VC], adj[b][:, j, cols], vhi[:, j, :],
                                         start=(j == 0), stop=False)
                        nc.tensor.matmul(bank[6 + i][:, 0:VC], adj[b][:, j, cols], vlo[:, j, :],
                                         start=False, stop=(j == NT - 1))
                    for j in range(NT):
                        if i == 0 and j % JH == 0:
                            pe.wait_ge(e_ready, chunk * 2 + j // JH + 1)
                        mm = nc.tensor.matmul(bank[4 + i][:, 0:D + 1], E[b][:, j, cols], haug[:, j, :],
                                              start=(j == 0), stop=(j == NT - 1))
                    mm.then_inc(rows_ready, 1)

            products(0, 0, 0)
            products(1, 1, 0)
            with pe.Fori(1, NCH // 2) as r:
                for b in range(2):
                    products(r * 2 + b, b, r)

        def rectify(act, chunk, b):
            for g in range(2):
                for j in range(g * JH, (g + 1) * JH):
                    ins = nc.scalar.activation(E[b][:, j, :], sleft[:, bass.ds(chunk * CH, CH)], ACT.Relu,
                                               bias=extra[:, j, 1:2])
                ins.then_inc(relu_ready, 1)

        def exponentiate(act, chunk, b):
            for g in range(2):
                act.wait_ge(lin_ready, chunk * 2 + g + 1)
                for j in range(g * JH, (g + 1) * JH):
                    ins = nc.scalar.activation(E[b][:, j, :], E[b][:, j, :], ACT.Exp, scale=-0.01,
                                               bias=negright[:, j:j + 1])
                ins.then_inc(exp_ready, 1)

        def squashes(act, chunk):
            for i in range(IT):
                t = chunk * IT + i
                act.wait_ge(gate_ready, t + 1)
                nc.scalar.activation(gatet[:, :], gate[:, :], ACT.Tanh, scale=0.5).then_inc(gate_squashed, 1)
                act.wait_ge(mix_ready, t + 1)
                nc.scalar.activation(squash[:, :], mixed[:, :], ACT.Tanh, scale=0.5).then_inc(mix_squashed, 1)

        @block.scalar
        def _(act):
            n = 0
            for g in range(NTG):
                for c in range(DC):
                    act.wait_ge(tr_ready, n + 1)
                    nc.scalar.copy(xnT[:, c, g * TG * P:(g + 1) * TG * P], bank[n % 2][:, :]).then_inc(tr_copied, 1)
                    n += 1
            for q in range(N // 512):
                act.wait_ge(sl_ready, q + 1)
                nc.scalar.copy(sleft[:, q * 512:(q + 1) * 512], bank[q % 2][:, :]).then_inc(sl_copied, 1)
            for t in range(NT):
                act.wait_ge(hv_ready, t + 1)
                nc.scalar.copy(haug[:, t, 0:D], bank[4 + t % 2][:, 0:D])
                nc.scalar.copy(extra[:, t, :], bank[4 + t % 2][:, D:HC]).then_inc(h_copied, 1)
            act.wait_ge(h_copied, NT)
            act.wait_ge(sl_copied, N // 512)
            for b in range(2):
                rectify(act, b, b)
                if b == 0:
                    act.wait_ge(negright_ready, 1)
                exponentiate(act, b, b)
            with act.Fori(0, NCH // 2 - 1) as r:
                for b in range(2):
                    squashes(act, r * 2 + b)
                    act.wait_ge(rows_ready, r * (2 * IT) + (b + 1) * IT)
                    rectify(act, r * 2 + 2 + b, b)
                    exponentiate(act, r * 2 + 2 + b, b)
            for b in range(2):
                squashes(act, NCH - 2 + b)

        def linear(dve, chunk, b):
            for g in range(2):
                dve.wait_ge(relu_ready, chunk * 2 + g + 1)
                part = E[b][:, g * JH:(g + 1) * JH, :]
                row = sleft[:, bass.ds(chunk * CH, CH)].unsqueeze(1).to_broadcast([P, JH, CH])
                nc.vector.scalar_tensor_tensor(out=part, in0=part, scalar=99.0, in1=row, op0=ALU.mult, op1=ALU.add)\
                    .then_inc(lin_ready, 1)

        def mask(dve, chunk, b, rnd):
            dve.wait_ge(adj_loaded[b], rnd * 16 + 16)
            for g in range(2):
                dve.wait_ge(exp_ready, chunk * 2 + g + 1)
                part = slice(g * JH, (g + 1) * JH)
                nc.vector.scalar_tensor_tensor(out=E[b][:, part, :], in0=E[b][:, part, :], scalar=BIG,
                                               in1=adj[b][:, part, :].bitcast(F32), op0=ALU.min, op1=ALU.mult)\
                    .then_inc(e_ready, 1)

        def combine(dve, chunk):
            STEPS = 8
            for i in range(IT):
                t = chunk * IT + i
                step = Tally(post_step, t * STEPS)
                X, V = bank[4 + i], bank[6 + i]
                dve.wait_ge(rows_ready, t + 1)
                step.link(dve, nc.vector.tensor_tensor(
                    gate[:, :], V[:, D:VC], extra[:, bass.ds(t, 1), 2:4].squeeze(1), ALU.add))
                nc.vector.tensor_tensor(gate[:, :], gate[:, :], bab[:, :], ALU.add).then_inc(gate_ready, 1)
                step.link(dve, nc.vector.tensor_scalar(rowsum[:, :], X[:, D:D + 1], 1e-5, None, ALU.add))
                step.link(dve, nc.vector.reciprocal(rinv[:, :], rowsum[:, :]))
                step.link(dve, nc.vector.tensor_tensor(xb[:, :], V[:, 0:D], bg[:, :], ALU.add))
                dve.wait_ge(gate_squashed, t + 1)
                step.link(dve, nc.vector.tensor_scalar(gates[:, :], gatet[:, :], 0.5, 0.5, ALU.mult, ALU.add))
                step.link(dve, nc.vector.tensor_tensor(coef[:, :], gates[:, 0:1], rinv[:, :], ALU.mult))
                step.link(dve, nc.vector.tensor_scalar(xb2[:, :], xb[:, :], gates[:, 1:2], None, ALU.mult))
                nc.vector.scalar_tensor_tensor(out=mixed[:, :], in0=X[:, 0:D], scalar=coef[:, 0:1],
                                               in1=xb2[:, :], op0=ALU.mult, op1=ALU.add).then_inc(mix_ready, 1)
                row = x_sb[:, bass.ds(t, 1), :].squeeze(1)
                step.link(dve, nc.vector.tensor_scalar(half[:, :], row, 0.5, None, ALU.add))
                dve.wait_ge(mix_squashed, t + 1)
                nc.vector.scalar_tensor_tensor(out=row, in0=squash[:, :], scalar=0.5, in1=half[:, :],
                                               op0=ALU.mult, op1=ALU.add)
                assert step.n == STEPS

        @block.vector
        def _(dve):
            step = Tally(prep_step)
            nc.vector.memset(haug[:, :, D:D + 1], 1.0)
            step.link(dve, nc.vector.memset(ones[:, :], 1.0))
            for g in range(2):
                dve.wait_ge(x_loaded, 32)
                for t in range(g * NT // 2, (g + 1) * NT // 2):
                    last = nc.vector.bn_stats(stats[:, t, :], x_sb[:, t, :])
            step.link(dve, last)
            for t in range(NT):
                last = nc.vector.bn_aggr(meanvar[:, t, :], stats[:, t, :])
            step.link(dve, last)
            nc.vector.memset(mhalf[:, :], -0.5)
            nc.vector.tensor_scalar(varc[:, :], meanvar[:, :, 1:2].squeeze(2), 1e-5, None, ALU.add)\
                .then_inc(var_ready, 1)
            dve.wait_ge(rstd_ready, 1)
            for t in range(NT):
                nc.vector.tensor_scalar(xn[:, t, :], x_sb[:, t, :], meanvar[:, t, 0:1], rstd[:, t:t + 1],
                                        ALU.subtract, ALU.mult).then_inc(xn_ready, 1)
            dve.wait_ge(w_loaded, 16 * NW)
            dve.wait_ge(u_ready, 1)
            for c in range(DC):
                nc.vector.tensor_copy(wcatH[:, c, D:D + 2], bank[2][:, 2 * c:2 * c + 2])
            nc.vector.tensor_copy(wcatH[:, :, D + 2:D + 4], wab[:, :, 1, :])
            step.link(dve, nc.vector.tensor_copy(wcatV[:, :, D:D + 2], wab[:, :, 0, :]))
            for c in range(DC):
                last = nc.vector.tensor_scalar(uleft[:, c, :], ones[:, :], wcatH[:, c, D:D + 1], None, ALU.mult)
            last.then_inc(wcat_ready, 1)
            for t in range(NT):
                dve.wait_ge(hv_ready, t + 1)
                step.link(dve, nc.vector.tensor_copy(vhi[:, t, :], bank[6 + t % 2][:, 0:VC]))
                nc.vector.tensor_tensor(vlo[:, t, :], bank[6 + t % 2][:, 0:VC], vhi[:, t, :].bitcast(F32),
                                        ALU.subtract).then_inc(v_split, 1)
            dve.wait_ge(h_copied, NT)
            nc.vector.tensor_scalar(negright[:, :], extra[:, :, 1:2].squeeze(2), -0.01, None, ALU.mult)\
                .then_inc(negright_ready, 1)
            for b in range(2):
                linear(dve, b, b)
                mask(dve, b, b, 0)
            with dve.Fori(0, NCH // 2 - 1) as r:
                for b in range(2):
                    combine(dve, r * 2 + b)
                    linear(dve, r * 2 + 2 + b, b)
                    mask(dve, r * 2 + 2 + b, b, r + 1)
            for b in range(2):
                combine(dve, NCH - 2 + b)
            nc.vector.memset(gate[:, :], 0.0).then_inc(x2_written, 1)


def ode_stage(nc, W1T_d, W2T_d, W3T_d, b1_d, b2_d, b3_d, G_d, out_d, x_sb, ident, ones):
    D, H = W1T_d.shape
    N = out_d.shape[0]
    T = P
    S = 3 * T
    NWIN = N // T
    DC, HC = D // P, H // P
    dt = 1.0 / (N - 1)
    TOL = 2.0 ** -17
    CAP = T + 4
    NTILE = 2 * HC
    RING = 4
    NB = 6
    GRP = 4

    order = []
    for lo, hi in ((0, HC), (HC, HC + GRP)):
        for t in range(lo, hi):
            order.append(("s", t))
            if t > lo:
                order.append(("d", t - 1))
        order.append(("d", hi - 1))
    for t in range(HC + GRP, NTILE):
        order += [("s", t), ("d", t)]

    with ExitStack() as ctx:
        def sb(name, shape, dt_=F32):
            return ctx.enter_context(nc.sbuf_tensor(name, shape, dt_))

        def sem(name):
            return ctx.enter_context(nc.semaphore(name))

        bank = [ctx.enter_context(nc.psum_tensor(f"obank{i}", [P, 512], F32)) for i in range(8)]
        W1 = sb("W1", [P, DC, H])
        W2 = sb("W2", [P, HC, H])
        W3 = sb("W3", [P, HC, D])
        W1r = sb("W1r", [P, DC, H], F32R)
        W2r = sb("W2r", [P, HC, H], F32R)
        W3r = sb("W3r", [P, HC, D], F32R)
        bias = sb("bias", [P, 2, HC])
        bias3 = sb("bias3", [P, DC])
        G = sb("G", [P, 2 * T])
        Y = sb("Y", [P, DC, T])
        dZ = sb("dZ", [P, DC, S], F32R)
        hid = sb("hid", [P, 2, HC, T])
        dhid = sb("dhid", [P, 2, HC, S], F32R)
        base = sb("base", [P, RING, T])
        pre = sb("pre", [P, RING, S])
        squ = sb("squ", [P, RING, S])
        K = sb("K", [P, DC, 4 * T])
        ka = sb("ka", [P, DC, T])
        kb = sb("kb", [P, DC, T])
        inc = sb("inc", [P, DC, T])
        traj = sb("traj", [P, DC, T + 1])
        diff = sb("diff", [P, 2, DC, T])
        worst = sb("worst", [P, 1])
        okay = sb("okay", [P, 1])
        rounds = sb("rounds", [1, 1])
        capped = sb("capped", [1, 1])
        flag = sb("flag", [1, 1], I32)
        incT = sb("incT", [P, D])
        rows = sb("rows", [P, D])
        stat = sb("stat", [1, 8])
        row0 = sb("row0", [1, D])
        ycol = sb("ycol", [P, DC])

        w_in = sem("w_in")
        w_rounded = sem("w_rounded")
        var0_ready = sem("var0_ready")
        rstd0_ready = sem("rstd0_ready")
        row0_ready = sem("row0_ready")
        y0_ready = sem("y0_ready")
        init_step = sem("init_step")
        guess_y = sem("guess_y")
        guess_dz = sem("guess_dz")
        y_next = sem("y_next")
        dz_next = sem("dz_next")
        pre_ready = sem("pre_ready")
        hid_ready = sem("hid_ready")
        sum_ready = sem("sum_ready")
        squ_ready = sem("squ_ready")
        dhid_ready = sem("dhid_ready")
        k_ready = sem("k_ready")
        K_written = sem("K_written")
        inc_ready = sem("inc_ready")
        traj_ready = sem("traj_ready")
        dz_checked = sem("dz_checked")
        tail_step = sem("tail_step")
        okay_ready = sem("okay_ready")
        votes_ready = sem("votes_ready")
        flag_ready = sem("flag_ready")
        flag_seen = sem("flag_seen")
        flag_read = sem("flag_read")
        turned = sem("turned")
        incT_ready = sem("incT_ready")
        guess_sum = sem("guess_sum")
        rounds_cleared = sem("rounds_cleared")
        start_moved = sem("start_moved")
        rows_out = sem("rows_out")
        stored = sem("stored")

        NLOAD = 7
        votes = bank[6][0:1, 0:1]
        block = ctx.enter_context(nc.Block())

        def read_flag(eng, n, stop, engine_flag_reads):
            eng.wait_ge(flag_ready, n + 1)
            eng.sem_inc(flag_seen, 1)
            eng.reg_load(stop, flag[0:1, 0:1]).then_inc(flag_read, 1)

        @block.sync
        def _(sp):
            sp.dma_start(W1[:, :, :], W1T_d.rearrange("(c p) h -> p c h", p=P)).then_inc(w_in, 16)
            sp.dma_start(bias[:, 0, :], b1_d).then_inc(w_in, 16)
            sp.dma_start(bias[:, 1, :], b2_d).then_inc(w_in, 16)
            sp.dma_start(bias3[:, :], b3_d).then_inc(w_in, 16)
            sp.dma_start(G[:, :], G_d).then_inc(w_in, 16)
            sp.dma_start(W2[:, :, :], W2T_d.rearrange("(c p) h -> p c h", p=P)).then_inc(w_in, 16)
            sp.dma_start(W3[:, :, :], W3T_d.rearrange("(c p) h -> p c h", p=P)).then_inc(w_in, 16)
            sp.sem_inc(stored, 16)
            with sp.Fori(0, NWIN) as w:
                sp.wait_ge(rows_out, w + 1)
                sp.dma_start(out_d[bass.ds(w * T, T), :], rows[:, :]).then_inc(stored, 16)
            sp.wait_ge(stored, 16 * NWIN + 16)

        @block.gpsimd
        def _(pool):
            pool.wait_ge(var0_ready, 1)
            nc.gpsimd.tensor_tensor(stat[0:1, 2:3], stat[0:1, 0:1], stat[0:1, 1:2], ALU.pow).then_inc(rstd0_ready, 1)

        @block.tensor
        def _(pe):
            pe.wait_ge(row0_ready, 1)
            for c in range(DC):
                mm = nc.tensor.matmul(bank[7][:, c:c + 1], row0[0:1, c * P:(c + 1) * P], ones[0:1, 0:1],
                                      start=True, stop=True)
            mm.then_inc(y0_ready, 1)
            pe.wait_ge(w_rounded, 3)
            rnd = pe.alloc_register("pe_round")
            stop = pe.alloc_register("pe_stop")
            pe.reg_mov(rnd, 0)
            pe.sem_inc(flag_read, 1)
            with pe.Fori(0, NWIN) as w:
                pe.reg_mov(stop, 0)
                pe.wait_ge(guess_y, w + 1)
                pe.wait_ge(guess_dz, w + 1)
                with pe.While(lambda: pe.snap(stop) == 0):
                    n = pe.snap(rnd)
                    pe.wait_ge(y_next, n + 1)
                    pe.wait_ge(dz_next, n + 1)

                    def bank_free(t):
                        if t >= NB:
                            pe.wait_ge(sum_ready, n * NTILE + (t - NB + 1))

                    def product(t, w_full, w_round, cols, k, last_k, x, dx):
                        A = bank[t % NB]
                        nc.tensor.matmul(A[:, 0:T], w_full[:, k, cols], x, start=(k == 0), stop=(k == last_k),
                                         skip_group_check=True)
                        return nc.tensor.matmul(A[:, T:4 * T], w_round[:, k, cols], dx, start=False,
                                                stop=(k == last_k), skip_group_check=True)

                    for m in range(HC):
                        bank_free(m)
                        for k in range(DC):
                            mm = product(m, W1, W1r, slice(m * P, (m + 1) * P), k, DC - 1, Y[:, k, :], dZ[:, k, :])
                        mm.then_inc(pre_ready, 1)
                    for m in range(GRP):
                        bank_free(HC + m)
                    for k in range(HC):
                        pe.wait_ge(dhid_ready, n * NTILE + k + 1)
                        for m in range(GRP):
                            mm = product(HC + m, W2, W2r, slice(m * P, (m + 1) * P), k, HC - 1,
                                         hid[:, 0, k, :], dhid[:, 0, k, :])
                            if k == HC - 1:
                                mm.then_inc(pre_ready, 1)
                    for m in range(GRP, HC):
                        bank_free(HC + m)
                        for k in range(HC):
                            mm = product(HC + m, W2, W2r, slice(m * P, (m + 1) * P), k, HC - 1,
                                         hid[:, 0, k, :], dhid[:, 0, k, :])
                        mm.then_inc(pre_ready, 1)
                    for c in range(DC):
                        bank_free(NTILE + c)
                    for k in range(HC):
                        pe.wait_ge(dhid_ready, n * NTILE + HC + k + 1)
                        for c in range(DC):
                            mm = product(NTILE + c, W3, W3r, slice(c * P, (c + 1) * P), k, HC - 1,
                                         hid[:, 1, k, :], dhid[:, 1, k, :])
                    mm.then_inc(k_ready, 1)
                    pe.wait_ge(okay_ready, n + 1)
                    nc.tensor.matmul(votes, okay[:, :], ones[:, 0:1], start=True, stop=True).then_inc(votes_ready, 1)
                    pe.reg_add(rnd, rnd, 1)
                    read_flag(pe, n, stop, flag_read)
                for c in range(DC):
                    nc.tensor.transpose(bank[7][:, c * P:(c + 1) * P], inc[:, c, :], ident[:, :])
                for c in range(DC):
                    mm = nc.tensor.transpose(bank[7][:, D + c * P:D + (c + 1) * P], traj[:, c, 0:T], ident[:, :])
                mm.then_inc(turned, 1)
                pe.wait_ge(incT_ready, w + 1)
                for c in range(DC):
                    mm = nc.tensor.matmul(bank[6][:, c * 2 * T:(c + 1) * 2 * T], incT[:, c * P:(c + 1) * P], G[:, :],
                                          start=True, stop=True)
                mm.then_inc(guess_sum, 1)

        @block.scalar
        def _(act):
            act.wait_ge(w_in, 16 * NLOAD)
            nc.scalar.copy(W2r[:, 0:HC // 2, :], W2[:, 0:HC // 2, :]).then_inc(w_rounded, 1)
            rnd = act.alloc_register("act_round")
            stop = act.alloc_register("act_stop")
            act.reg_mov(rnd, 0)
            act.sem_inc(flag_read, 1)
            act.sem_inc(dz_next, 1)
            with act.Fori(0, NWIN) as w:
                act.reg_mov(stop, 0)
                with act.While(lambda: act.snap(stop) == 0):
                    n = act.snap(rnd)
                    for what, t in order:
                        layer, m, slot = t // HC, t % HC, t % RING
                        b = bias[:, layer, m:m + 1]
                        A = bank[t % NB]
                        if what == "s":
                            act.wait_ge(pre_ready, n * NTILE + t + 1)
                            if t >= RING:
                                act.wait_ge(sum_ready, n * NTILE + t - RING + 1)
                            nc.scalar.activation(base[:, slot, :], A[:, 0:T], ACT.Identity, bias=b)
                            nc.scalar.activation(hid[:, layer, m, :], A[:, 0:T], ACT.Tanh, bias=b)\
                                .then_inc(hid_ready, 1)
                        else:
                            act.wait_ge(sum_ready, n * NTILE + t + 1)
                            if t >= RING:
                                act.wait_ge(dhid_ready, n * NTILE + t - RING + 1)
                            nc.scalar.activation(squ[:, slot, :], pre[:, slot, :], ACT.Tanh).then_inc(squ_ready, 1)
                    act.wait_ge(K_written, n + 1)
                    act.wait_ge(dz_checked, n + 1)
                    nc.scalar.mul(dZ[:, :, 0:2 * T], K[:, :, 0:2 * T], dt / 2)
                    nc.scalar.mul(dZ[:, :, 2 * T:S], K[:, :, 2 * T:S], dt).then_inc(dz_next, 1)
                    act.reg_add(rnd, rnd, 1)
                    read_flag(act, n, stop, flag_read)
                act.wait_ge(turned, w + 1)
                nc.scalar.copy(incT[:, :], bank[7][:, 0:D]).then_inc(incT_ready, 1)
                act.wait_ge(guess_y, w + 2)
                for c in range(DC):
                    g = bank[6][:, c * 2 * T + T:(c + 1) * 2 * T]
                    nc.scalar.mul(dZ[:, c, 0:T], g, 0.5)
                    nc.scalar.mul(dZ[:, c, T:2 * T], g, 0.5)
                    last = nc.scalar.copy(dZ[:, c, 2 * T:S], g)
                last.then_inc(guess_dz, 1)

        @block.vector
        def _(dve):
            step = Tally(init_step)
            step.link(dve, nc.vector.bn_stats(stat[0:1, 0:6], x_sb[0:1, 0, :]))
            step.link(dve, nc.vector.bn_aggr(stat[0:1, 6:8], stat[0:1, 0:6]))
            nc.vector.memset(stat[0:1, 1:2], -0.5)
            nc.vector.tensor_scalar(stat[0:1, 0:1], stat[0:1, 7:8], 1e-5, None, ALU.add).then_inc(var0_ready, 1)
            dve.wait_ge(rstd0_ready, 1)
            nc.vector.tensor_scalar(row0[:, :], x_sb[0:1, 0, :], stat[0:1, 6:7], stat[0:1, 2:3],
                                    ALU.subtract, ALU.mult).then_inc(row0_ready, 1)
            dve.wait_ge(w_in, 16 * NLOAD)
            nc.vector.tensor_copy(W1r[:, :, :], W1[:, :, :])
            nc.vector.tensor_copy(W3r[:, :, :], W3[:, :, :]).then_inc(w_rounded, 1)
            nc.vector.tensor_copy(W2r[:, HC // 2:HC, :], W2[:, HC // 2:HC, :]).then_inc(w_rounded, 1)
            dve.wait_ge(y0_ready, 1)
            step.link(dve, nc.vector.tensor_copy(ycol[:, :], bank[7][:, 0:DC]))
            nc.vector.memset(dZ[:, :, :].bitcast(F32), 0.0).then_inc(guess_dz, 1)
            for c in range(DC):
                nc.vector.tensor_copy(traj[:, c, 0:1], ycol[:, c:c + 1])
            for c in range(DC):
                last = nc.vector.tensor_scalar(Y[:, c, :], ones[:, :], ycol[:, c:c + 1], None, ALU.mult)
            last.then_inc(guess_y, 1)
            rnd = dve.alloc_register("dve_round")
            stop = dve.alloc_register("dve_stop")
            dve.reg_mov(rnd, 0)
            dve.sem_inc(flag_read, 1)
            dve.sem_inc(y_next, 1)
            with dve.Fori(0, NWIN) as w:
                dve.reg_mov(stop, 0)
                nc.vector.memset(rounds[:, :], 0.0).then_inc(rounds_cleared, 1)
                with dve.While(lambda: dve.snap(stop) == 0):
                    n = dve.snap(rnd)
                    for what, t in order:
                        layer, m, slot = t // HC, t % HC, t % RING
                        A = bank[t % NB]
                        if what == "s":
                            dve.wait_ge(hid_ready, n * NTILE + t + 1)
                            if t >= RING:
                                dve.wait_ge(squ_ready, n * NTILE + t - RING + 1)
                            nc.vector.tensor_tensor(
                                pre[:, slot, :].rearrange("p (s t) -> p s t", t=T),
                                A[:, T:4 * T].rearrange("p (s t) -> p s t", t=T),
                                base[:, slot, :].unsqueeze(1).to_broadcast([P, 3, T]), ALU.add)\
                                .then_inc(sum_ready, 1)
                        else:
                            dve.wait_ge(squ_ready, n * NTILE + t + 1)
                            nc.vector.tensor_tensor(
                                dhid[:, layer, m, :].rearrange("p (s t) -> p s t", t=T),
                                squ[:, slot, :].rearrange("p (s t) -> p s t", t=T),
                                hid[:, layer, m, :].unsqueeze(1).to_broadcast([P, 3, T]), ALU.subtract)\
                                .then_inc(dhid_ready, 1)
                    TAIL = 9
                    tail = Tally(tail_step, n * TAIL)
                    dve.wait_ge(k_ready, n + 1)
                    for c in range(DC):
                        last = nc.vector.tensor_scalar(K[:, c, 0:T], bank[(NTILE + c) % NB][:, 0:T],
                                                       bias3[:, c:c + 1], None, ALU.add)
                    tail.link(dve, last)
                    for c in range(DC):
                        last = nc.vector.tensor_tensor(
                            K[:, c, T:4 * T].rearrange("p (s t) -> p s t", t=T),
                            bank[(NTILE + c) % NB][:, T:4 * T].rearrange("p (s t) -> p s t", t=T),
                            K[:, c, 0:T].unsqueeze(1).to_broadcast([P, 3, T]), ALU.add)
                    last.then_inc(K_written, 1)
                    dve.wait_ge(K_written, n + 1)
                    k = [K[:, :, s * T:(s + 1) * T] for s in range(4)]
                    nc.vector.scalar_tensor_tensor(out=ka[:, :, :], in0=k[1], scalar=2.0, in1=k[0],
                                                   op0=ALU.mult, op1=ALU.add)
                    tail.link(dve, nc.vector.scalar_tensor_tensor(out=kb[:, :, :], in0=k[2], scalar=2.0, in1=k[3],
                                                                  op0=ALU.mult, op1=ALU.add))
                    tail.link(dve, nc.vector.tensor_tensor(ka[:, :, :], ka[:, :, :], kb[:, :, :], ALU.add))
                    nc.vector.tensor_scalar(inc[:, :, :], ka[:, :, :], dt / 6, None, ALU.mult).then_inc(inc_ready, 1)
                    dve.wait_ge(inc_ready, n + 1)
                    for c in range(DC):
                        last = nc.vector.tensor_tensor_scan(traj[:, c, 1:T + 1], ones[:, :], inc[:, c, :],
                                                            traj[:, c, 0:1], ALU.mult, ALU.add)
                    nc.vector.scalar_tensor_tensor(out=diff[:, 1, :, :], in0=k[2], scalar=dt,
                                                   in1=dZ[:, :, 2 * T:S].bitcast(F32), op0=ALU.mult,
                                                   op1=ALU.subtract).then_inc(dz_checked, 1)
                    tail.link(dve, last)
                    tail.link(dve, nc.vector.tensor_tensor(diff[:, 0, :, :], traj[:, :, 0:T], Y[:, :, :],
                                                           ALU.subtract))
                    nc.vector.tensor_copy(Y[:, :, :], traj[:, :, 0:T]).then_inc(y_next, 1)
                    dve.wait_ge(dz_checked, n + 1)
                    tail.link(dve, nc.vector.tensor_reduce(worst[:, :], diff[:, :, :, :], AX.XYZ, ALU.max,
                                                           apply_absolute_value=True))
                    nc.vector.tensor_scalar(okay[:, :], worst[:, :], TOL, None, ALU.is_le).then_inc(okay_ready, 1)
                    dve.wait_ge(rounds_cleared, w + 1)
                    tail.link(dve, nc.vector.tensor_scalar(rounds[:, :], rounds[:, :], 1.0, None, ALU.add))
                    tail.link(dve, nc.vector.tensor_scalar(capped[:, :], rounds[:, :], float(CAP), None, ALU.is_ge))
                    dve.wait_ge(votes_ready, n + 1)
                    dve.wait_ge(flag_read, n * 3 + 3)
                    tail.link(dve, nc.vector.scalar_tensor_tensor(
                        out=kb[0:1, 0, 0:1], in0=votes, scalar=P - 0.5, in1=capped[:, :],
                        op0=ALU.is_ge, op1=ALU.max))
                    nc.vector.tensor_copy(flag[:, :], kb[0:1, 0, 0:1]).then_inc(flag_ready, 1)
                    assert tail.n == TAIL
                    dve.reg_add(rnd, rnd, 1)
                    read_flag(dve, n, stop, flag_read)
                dve.wait_ge(turned, w + 1)
                nc.vector.tensor_copy(traj[:, :, 0:1], traj[:, :, T:T + 1]).then_inc(start_moved, 1)
                dve.wait_ge(stored, w * 16 + 16)
                dve.wait_ge(incT_ready, w + 1)
                nc.vector.tensor_tensor(rows[:, :], bank[7][:, D:2 * D], x_sb[:, bass.ds(w, 1), :].squeeze(1),
                                        ALU.add).then_inc(rows_out, 1)
                dve.wait_ge(start_moved, w + 1)
                dve.wait_ge(guess_sum, w + 1)
                for c in range(DC):
                    last = nc.vector.tensor_scalar(Y[:, c, :], bank[6][:, c * 2 * T:c * 2 * T + T],
                                                   traj[:, c, 0:1], None, ALU.add)
                last.then_inc(guess_y, 1)


def build(nc, d, out):
    with ExitStack() as ctx:
        N, D = d["x"].shape
        x_sb = ctx.enter_context(nc.sbuf_tensor("x_sb", [P, N // P, D], F32))
        ident = ctx.enter_context(nc.sbuf_tensor("ident", [P, P], F32))
        ones = ctx.enter_context(nc.sbuf_tensor("ones", [P, P], F32))
        graph_stage(nc, d["x"], d["adjT"], d["WsaT"], d["Wsa"], d["a"], d["Wg"], d["bg"], d["wab"], d["bab"],
                    d["ident"], x_sb, ident, ones)
        ode_stage(nc, d["W1T"], d["W2T"], d["W3T"], d["b1"], d["b2"], d["b3"], d["G"], out, x_sb, ident, ones)


def guess_table(T, degree):
    import numpy as np
    past = (2 * np.arange(T) - 2 * T) / T + 1.0
    ahead = (2 * np.arange(T)) / T + 1.0
    fit = np.linalg.pinv(np.polynomial.chebyshev.chebvander(past, degree))
    value = fit.T @ np.polynomial.chebyshev.chebvander(ahead, degree).T
    summed = np.concatenate([np.zeros((T, 1)), np.cumsum(value, axis=1)[:, :-1]], axis=1)
    return np.concatenate([summed, value], axis=1).astype(np.float32)


def kernel(**inputs):
    import numpy as np
    import concourse.bacc as bacc
    from concourse.bass_utils import run_bass_kernel_spmd as run

    g = {k: np.asarray(v) for k, v in inputs.items()}
    D = g["x"].shape[1]
    DC = D // P
    a = g["L0_gnn_a_sa"].reshape(2, DC, P).transpose(2, 1, 0)
    wab = np.stack([g["L0_gnn_Wa"][0], g["L0_gnn_Wb"][0]]).reshape(2, 2, DC, P).transpose(3, 2, 1, 0)
    bab = np.broadcast_to(np.concatenate([g["L0_gnn_ba"], g["L0_gnn_bb"]])[None], (P, 2))
    arrays = {
        "x": g["x"], "adjT": g["adj"].T, "WsaT": g["L0_gnn_W_sa"].T, "Wsa": g["L0_gnn_W_sa"], "a": a,
        "Wg": g["L0_gnn_W_gcnb"], "bg": np.broadcast_to(g["L0_gnn_b_gcnb"][None], (P, D)), "wab": wab, "bab": bab,
        "ident": np.eye(P, dtype=np.float32),
        "W1T": g["L0_ffn_W1"].T, "W2T": g["L0_ffn_W2"].T, "W3T": g["L0_ffn_W3"].T,
        "b1": g["L0_ffn_b1"].reshape(-1, P).T, "b2": g["L0_ffn_b2"].reshape(-1, P).T,
        "b3": g["L0_ffn_b3"].reshape(-1, P).T, "G": guess_table(P, 5),
    }
    arrays = {f"in_{k}": np.ascontiguousarray(v) for k, v in arrays.items()}
    nc = bacc.Bacc("TRN2", target_bir_lowering=False, num_devices=1)
    d = {k[3:]: nc.dram_tensor(k, v.shape, mybir.dt.from_np(v.dtype), kind="ExternalInput").ap()
         for k, v in arrays.items()}
    out = nc.dram_tensor("out_y", g["x"].shape, F32, kind="ExternalOutput").ap()
    build(nc, d, out)
    return run(nc, [arrays], core_ids=[0]).results[0]["out_y"]
```
